# Optimizing a Trainium2 kernel written in Bass

```python
import numpy as np
import jax
import jax.numpy as jnp

def _softmax(x, axis=-1):
    return jax.nn.softmax(x, axis=axis)

def _gelu(x):
    return jax.nn.gelu(x, approximate=True)

def _silu(x):
    return jax.nn.silu(x)

def _sigmoid(x):
    return jax.nn.sigmoid(x)

def _layernorm(x, axis=-1, eps=1e-05):
    m = jnp.mean(x, axis=axis, keepdims=True)
    v = jnp.var(x, axis=axis, keepdims=True)
    return (x - m) / jnp.sqrt(v + eps)

def _scatter_add(tgt, idx, src, axis=0):
    return tgt.at[idx].add(src)

def _segment_sum(src, seg, n):
    return jax.ops.segment_sum(src, seg, n)
kernel_name = 'mk_xattn_ffn_d2_seqx_r8_188b6d'

def setup_inputs(seed: int=0):
    np.random.seed(seed)
    _w = jnp.asarray

    def _rec_inputs():
        import jax
        import jax.numpy as jnp
        _rk = jax.random.key(seed)
        x = -0.000125 + 0.9999 * jax.random.normal(jax.random.fold_in(_rk, 1), (4, 256, 256), jnp.float32)
        _lenS = 256 - jax.random.randint(jax.random.fold_in(_rk, 7), (4,), 0, max(1, 256 // 4) + 1, jnp.int32)
        _lenS2 = 256 - jax.random.randint(jax.random.fold_in(_rk, 8), (4,), 0, max(1, 256 // 4) + 1, jnp.int32)
        itok_BxS_13_99985 = jax.random.randint(jax.random.fold_in(_rk, 11), (4, 256), 13, 99986, jnp.int32)
        _ctx_2048P = jax.random.normal(jax.random.fold_in(_rk, 12), (4, 16, 256), jnp.float32)
        _ctx_2048c = jax.random.dirichlet(jax.random.fold_in(_rk, 512), 0.3 * jnp.ones((16,), jnp.float32), (4, 256))
        _ctx_2048t = jnp.einsum('bsk,bkd->bsd', _ctx_2048c, _ctx_2048P)
        _ctx_2048t = _ctx_2048t * jax.lax.rsqrt(jnp.mean(jnp.square(_ctx_2048t)) + 1e-12) * 0.953939
        ctx_2048 = 6.82029e-06 + 0.0200006 * (_ctx_2048t + 0.3 * jax.random.normal(jax.random.fold_in(_rk, 612), (4, 256, 256), jnp.float32))
        return (x, itok_BxS_13_99985, ctx_2048)
    x, itok_BxS_13_99985, ctx_2048 = _rec_inputs()

    def _L0_xattn_setup():
        import jax, jax.numpy as jnp
        import numpy as np
        B, S, D = (4, 512, 256)
        E = 4
        F = 1024 // E
        VOCAB = 12500
        key = jax.random.key(seed)
        k1, k2, k3, k4, k5 = jax.random.split(key, 5)
        hidden_states = jax.random.normal(k1, (B, S, D), dtype=jnp.float32)
        token_ids = jax.random.randint(k2, (B, S), 0, VOCAB, dtype=jnp.int64)
        Wg = jax.random.normal(k3, (E, F, D), dtype=jnp.float32) * 0.02
        Wu = jax.random.normal(k4, (E, F, D), dtype=jnp.float32) * 0.02
        Wd = jax.random.normal(k5, (E, D, F), dtype=jnp.float32) * 0.02
        return {'hidden_states': hidden_states, 'token_ids': token_ids, 'Wg': Wg, 'Wu': Wu, 'Wd': Wd}
    _L0_xattn_all = _L0_xattn_setup()
    _L0_xattn_in = {k: v for k, v in _L0_xattn_all.items() if k in ()}
    del _L0_xattn_all

    def _L0_ffn_setup():
        import jax, jax.numpy as jnp
        import numpy as np
        B, S, HID = (2, 256, 256)
        NUM_HEADS = 16
        HEAD_DIM = HID // NUM_HEADS
        NUM_EXPERTS = 8
        TOP_K = 2
        INTER = 512
        EPS = 1e-05

        def _rmsnorm(x, w, eps=EPS):
            return x * jax.lax.rsqrt(jnp.mean(x * x, axis=-1, keepdims=True) + eps) * w

        def _moe(x_flat, Wr, Wg, Wu, Wd):
            T = x_flat.shape[0]
            logits = x_flat @ Wr.T
            top_logits, top_idx = jax.lax.top_k(logits, TOP_K)
            probs = jax.nn.softmax(top_logits, axis=-1)
            cw = jnp.zeros((T, NUM_EXPERTS), x_flat.dtype)
            cw = cw.at[jnp.arange(T)[:, None], top_idx].add(probs)
            hg = jnp.einsum('eih,th->eti', Wg, x_flat)
            hu = jnp.einsum('eih,th->eti', Wu, x_flat)
            y = jnp.einsum('ehi,eti->eth', Wd, jax.nn.silu(hg) * hu)
            return jnp.einsum('eth,te->th', y, cw)
        key = jax.random.key(seed)
        ks = jax.random.split(key, 12)
        sd_h = 1.0 / np.sqrt(HID)
        sd_i = 1.0 / np.sqrt(INTER)
        return {'x': jax.random.normal(ks[0], (B, S, HID), jnp.float32), 'Wq': jax.random.normal(ks[1], (HID, HID), jnp.float32) * sd_h, 'Wk': jax.random.normal(ks[2], (HID, HID), jnp.float32) * sd_h, 'Wv': jax.random.normal(ks[3], (HID, HID), jnp.float32) * sd_h, 'Wo': jax.random.normal(ks[4], (HID, HID), jnp.float32) * sd_h, 'w_ln1': jnp.ones((HID,), jnp.float32), 'w_ln2': jnp.ones((HID,), jnp.float32), 'Wr': jax.random.normal(ks[5], (NUM_EXPERTS, HID), jnp.float32) * sd_h, 'Wg': jax.random.normal(ks[6], (NUM_EXPERTS, INTER, HID), jnp.float32) * sd_h, 'Wu': jax.random.normal(ks[7], (NUM_EXPERTS, INTER, HID), jnp.float32) * sd_h, 'Wd': jax.random.normal(ks[8], (NUM_EXPERTS, HID, INTER), jnp.float32) * sd_i}
    _L0_ffn_all = _L0_ffn_setup()
    _L0_ffn_in = {k: v for k, v in _L0_ffn_all.items() if k in ('Wq', 'Wk', 'Wv', 'Wo', 'w_ln1', 'w_ln2', 'Wr', 'Wg', 'Wu', 'Wd')}
    del _L0_ffn_all

    def _L1_xattn_setup():
        import jax, jax.numpy as jnp
        import numpy as np
        B_DIM, T_DIM, C_DIM = (16, 128, 256)

        def _wkv(w, u, k, v):
            Bn, Tn, Cn = k.shape
            NEG_INF = jnp.float32(-1e+38)

            def step(carry, kv_t):
                p, q, o = carry
                kt, vt = kv_t
                no = jnp.maximum(o, u + kt)
                A = jnp.exp(o - no)
                E = jnp.exp(u + kt - no)
                y = (A * p + E * vt) / (A * q + E)
                no2 = jnp.maximum(w + o, kt)
                A2 = jnp.exp(w + o - no2)
                E2 = jnp.exp(kt - no2)
                return ((A2 * p + E2 * vt, A2 * q + E2, no2), y)
            init = (jnp.zeros((Bn, Cn), k.dtype), jnp.zeros((Bn, Cn), k.dtype), jnp.full((Bn, Cn), NEG_INF, k.dtype))
            kT = jnp.moveaxis(k, 1, 0)
            vT = jnp.moveaxis(v, 1, 0)
            _, yT = jax.lax.scan(step, init, (kT, vT))
            return jnp.moveaxis(yT, 0, 1)
        key = jax.random.key(seed)
        k1, k2, k3, k4 = jax.random.split(key, 4)
        w = -jnp.exp(jax.random.normal(k1, (C_DIM,), jnp.float32))
        u = jax.random.normal(k2, (C_DIM,), jnp.float32)
        k = jax.random.normal(k3, (B_DIM, T_DIM, C_DIM), jnp.float32)
        v = jax.random.normal(k4, (B_DIM, T_DIM, C_DIM), jnp.float32)
        return {'B': B_DIM, 'T': T_DIM, 'C': C_DIM, 'w': w, 'u': u, 'k': k, 'v': v}
    _L1_xattn_all = _L1_xattn_setup()
    _L1_xattn_in = {k: v for k, v in _L1_xattn_all.items() if k in ('w', 'u')}
    del _L1_xattn_all

    def _L1_ffn_setup():
        import jax, jax.numpy as jnp
        import numpy as np
        EPS = 1e-05

        def activation_quant(x):
            scale = 127.0 / jnp.clip(jnp.max(jnp.abs(x), axis=-1, keepdims=True), EPS, None)
            return jnp.clip(jnp.round(x * scale), -128.0, 127.0) / scale

        def weight_quant(w):
            scale = 1.0 / jnp.clip(jnp.mean(jnp.abs(w)), EPS, None)
            return jnp.clip(jnp.round(w * scale), -1.0, 1.0) / scale

        def bitlinear(x, w):
            xq = x + jax.lax.stop_gradient(activation_quant(x) - x)
            wq = w + jax.lax.stop_gradient(weight_quant(w) - w)
            return jnp.einsum('bsd,hd->bsh', xq, wq)
        key = jax.random.key(seed)
        k1, k2, k3 = jax.random.split(key, 3)
        B, S, D, H = (4, 256, 256, 1024)
        x = jax.random.normal(k1, (B, S, D), dtype=jnp.float32)
        w1 = jax.random.normal(k2, (H, D), dtype=jnp.float32) * 0.02
        w2 = jax.random.normal(k3, (D, H), dtype=jnp.float32) * 0.02
        return {'x': x, 'w1': w1, 'w2': w2}
    _L1_ffn_all = _L1_ffn_setup()
    _L1_ffn_in = {k: v for k, v in _L1_ffn_all.items() if k in ('w1', 'w2')}
    del _L1_ffn_all
    return {'x': x, 'itok_BxS_13_99985': itok_BxS_13_99985, 'ctx_2048': ctx_2048, 'L0_ffn_Wq': _L0_ffn_in['Wq'], 'L0_ffn_Wk': _L0_ffn_in['Wk'], 'L0_ffn_Wv': _L0_ffn_in['Wv'], 'L0_ffn_Wo': _L0_ffn_in['Wo'], 'L0_ffn_w_ln1': _L0_ffn_in['w_ln1'], 'L0_ffn_w_ln2': _L0_ffn_in['w_ln2'], 'L0_ffn_Wr': _L0_ffn_in['Wr'], 'L0_ffn_Wg': _L0_ffn_in['Wg'], 'L0_ffn_Wu': _L0_ffn_in['Wu'], 'L0_ffn_Wd': _L0_ffn_in['Wd'], 'L1_xattn_w': _L1_xattn_in['w'], 'L1_xattn_u': _L1_xattn_in['u'], 'L1_ffn_w1': _L1_ffn_in['w1'], 'L1_ffn_w2': _L1_ffn_in['w2']}

def reference(x, itok_BxS_13_99985, ctx_2048, L0_ffn_Wq, L0_ffn_Wk, L0_ffn_Wv, L0_ffn_Wo, L0_ffn_w_ln1, L0_ffn_w_ln2, L0_ffn_Wr, L0_ffn_Wg, L0_ffn_Wu, L0_ffn_Wd, L1_xattn_w, L1_xattn_u, L1_ffn_w1, L1_ffn_w2):
    import jax
    import jax.numpy as jnp

    def _L0_xattn_ref(hidden_states, token_ids, Wg, Wu, Wd):
        import jax, jax.numpy as jnp
        import numpy as np
        B, S, D = (4, 512, 256)
        E = 4
        F = 1024 // E
        VOCAB = 12500
        tokens_per_expert = VOCAB // E
        tid = jnp.clip(token_ids, 0, VOCAB - 1)
        expert_ids = jnp.minimum(tid // tokens_per_expert, E - 1)
        out = jnp.zeros_like(hidden_states)
        for e in range(E):
            g = jax.nn.silu(jnp.einsum('bsd,fd->bsf', hidden_states, Wg[e]))
            u = jnp.einsum('bsd,fd->bsf', hidden_states, Wu[e])
            y = jnp.einsum('bsf,df->bsd', g * u, Wd[e])
            out = jnp.where((expert_ids == e)[..., None], y, out)
        return out

    def _L0_ffn_ref(x, Wq, Wk, Wv, Wo, w_ln1, w_ln2, Wr, Wg, Wu, Wd):
        import jax, jax.numpy as jnp
        import numpy as np
        B, S, HID = (2, 256, 256)
        NUM_HEADS = 16
        HEAD_DIM = HID // NUM_HEADS
        NUM_EXPERTS = 8
        TOP_K = 2
        INTER = 512
        EPS = 1e-05

        def _rmsnorm(x, w, eps=EPS):
            return x * jax.lax.rsqrt(jnp.mean(x * x, axis=-1, keepdims=True) + eps) * w

        def _moe(x_flat, Wr, Wg, Wu, Wd):
            T = x_flat.shape[0]
            logits = x_flat @ Wr.T
            top_logits, top_idx = jax.lax.top_k(logits, TOP_K)
            probs = jax.nn.softmax(top_logits, axis=-1)
            cw = jnp.zeros((T, NUM_EXPERTS), x_flat.dtype)
            cw = cw.at[jnp.arange(T)[:, None], top_idx].add(probs)
            hg = jnp.einsum('eih,th->eti', Wg, x_flat)
            hu = jnp.einsum('eih,th->eti', Wu, x_flat)
            y = jnp.einsum('ehi,eti->eth', Wd, jax.nn.silu(hg) * hu)
            return jnp.einsum('eth,te->th', y, cw)
        b, s, hid = x.shape
        residual = x
        xn = _rmsnorm(x, w_ln1)
        q = (xn @ Wq.T).reshape(b, s, NUM_HEADS, HEAD_DIM)
        k = (xn @ Wk.T).reshape(b, s, NUM_HEADS, HEAD_DIM)
        v = (xn @ Wv.T).reshape(b, s, NUM_HEADS, HEAD_DIM)
        scale = 1.0 / np.sqrt(HEAD_DIM)
        attn = jnp.einsum('bqhd,bkhd->bhqk', q, k) * scale
        causal = jnp.tril(jnp.ones((s, s), bool))
        attn = jnp.where(causal[None, None], attn, -jnp.inf)
        attn = jax.nn.softmax(attn, axis=-1)
        h = jnp.einsum('bhqk,bkhd->bqhd', attn, v).reshape(b, s, hid)
        x = residual + h @ Wo.T
        residual = x
        xn = _rmsnorm(x, w_ln2)
        moe_out = _moe(xn.reshape(-1, hid), Wr, Wg, Wu, Wd).reshape(b, s, hid)
        return residual + moe_out

    def _L1_xattn_ref(B, T, C, w, u, k, v):
        import jax, jax.numpy as jnp
        import numpy as np
        B_DIM, T_DIM, C_DIM = (16, 128, 256)

        def _wkv(w, u, k, v):
            Bn, Tn, Cn = k.shape
            NEG_INF = jnp.float32(-1e+38)

            def step(carry, kv_t):
                p, q, o = carry
                kt, vt = kv_t
                no = jnp.maximum(o, u + kt)
                A = jnp.exp(o - no)
                E = jnp.exp(u + kt - no)
                y = (A * p + E * vt) / (A * q + E)
                no2 = jnp.maximum(w + o, kt)
                A2 = jnp.exp(w + o - no2)
                E2 = jnp.exp(kt - no2)
                return ((A2 * p + E2 * vt, A2 * q + E2, no2), y)
            init = (jnp.zeros((Bn, Cn), k.dtype), jnp.zeros((Bn, Cn), k.dtype), jnp.full((Bn, Cn), NEG_INF, k.dtype))
            kT = jnp.moveaxis(k, 1, 0)
            vT = jnp.moveaxis(v, 1, 0)
            _, yT = jax.lax.scan(step, init, (kT, vT))
            return jnp.moveaxis(yT, 0, 1)
        return _wkv(w, u, k, v)

    def _L1_ffn_ref(x, w1, w2):
        import jax, jax.numpy as jnp
        import numpy as np
        EPS = 1e-05

        def activation_quant(x):
            scale = 127.0 / jnp.clip(jnp.max(jnp.abs(x), axis=-1, keepdims=True), EPS, None)
            return jnp.clip(jnp.round(x * scale), -128.0, 127.0) / scale

        def weight_quant(w):
            scale = 1.0 / jnp.clip(jnp.mean(jnp.abs(w)), EPS, None)
            return jnp.clip(jnp.round(w * scale), -1.0, 1.0) / scale

        def bitlinear(x, w):
            xq = x + jax.lax.stop_gradient(activation_quant(x) - x)
            wq = w + jax.lax.stop_gradient(weight_quant(w) - w)
            return jnp.einsum('bsd,hd->bsh', xq, wq)
        h = bitlinear(x, w1)
        h = jax.nn.gelu(h, approximate=False)
        return bitlinear(h, w2)
    x = x + _L0_xattn_ref(_layernorm(x, axis=-1), itok_BxS_13_99985, ctx_2048, ctx_2048, ctx_2048)
    x = x + _L0_ffn_ref(_layernorm(x, axis=-1), L0_ffn_Wq, L0_ffn_Wk, L0_ffn_Wv, L0_ffn_Wo, L0_ffn_w_ln1, L0_ffn_w_ln2, L0_ffn_Wr, L0_ffn_Wg, L0_ffn_Wu, L0_ffn_Wd)
    x = x + _L1_xattn_ref(4, 256, 256, L1_xattn_w, L1_xattn_u, _layernorm(x, axis=-1), ctx_2048)
    x = x + _L1_ffn_ref(_layernorm(x, axis=-1), L1_ffn_w1, L1_ffn_w2)
    return x

_drawn_inputs = setup_inputs


def setup_inputs(seed=0):
    import zlib

    import numpy as np

    out = dict(_drawn_inputs(seed))
    spreads = {'L0_ffn_w_ln1': (1.0, 0.2), 'L0_ffn_w_ln2': (1.0, 0.2)}
    factors = {}
    for name, (base, spread) in spreads.items():
        noise = np.random.default_rng([zlib.crc32(name.encode()), seed]).standard_normal(out[name].shape)
        drawn = base * np.exp(spread * noise) if base else spread * noise
        out[name] = jnp.asarray(drawn.astype(out[name].dtype))
    for name, factor in factors.items():
        out[name] = (out[name] * factor).astype(out[name].dtype)
    return out
```

```python
import concourse.bass as bass
from concourse import mybir
from contextlib import ExitStack


def mixed_block_kernel(nc, x, ids, ctx_t, wqkv_t, wo_t, wr_t, wexp, ln1, ln2, decay, bonus, w1_t, w2_t, out):
    F = mybir.dt.float32
    R = mybir.dt.float32r
    BF = mybir.dt.bfloat16
    I32 = mybir.dt.int32
    U32 = mybir.dt.uint32
    ALU = mybir.AluOpType
    ACT = mybir.ActivationFunctionType
    AX = mybir.AxisListType.X

    P = 128
    D = 256
    KC = D // P
    N = x.shape[0]
    NT = N // P
    B = 4
    S = N // B
    TB = S // P
    NE_A = ctx_t.shape[1]
    H = 16
    HD = D // H
    NE = wexp.shape[0]
    INTER = 512
    IC = INTER // P
    WE = wexp.shape[2]
    NSLOT = (2 * N + NE * (P - 1)) // P
    NSE = NSLOT + NSLOT % 2
    F1 = w1_t.shape[2]
    FC = F1 // P
    EPS = 1e-5
    MAGIC = 12582912.0
    BIG = 1e30

    ctx = ExitStack()
    with ctx:
        base = ctx.enter_context(ExitStack())

        def sb(scope, name, shape, dt=F):
            return scope.enter_context(nc.sbuf_tensor(name, shape, dt))

        def sem(name):
            return ctx.enter_context(nc.semaphore(name))

        x_sb = sb(base, "x_sb", [P, NT, D])
        res = sb(base, "res", [P, NT, D])
        ctx_sb = sb(base, "ctx_sb", [P, KC, NE_A * D])
        h_t = sb(base, "h_t", [P, KC, N])
        wqkv = sb(base, "wqkv", [P, KC, 3 * D])
        wo = sb(base, "wo", [P, KC, D])
        wr = sb(base, "wr", [P, KC, NE])
        w1q = sb(base, "w1q", [P, KC, F1], BF)
        w2q = sb(base, "w2q", [P, FC, D], BF)
        ident = sb(base, "ident", [P, P])
        ident_b = sb(base, "ident_b", [P, P], BF)
        earlier = sb(base, "earlier", [P, P], BF)
        ones_b = sb(base, "ones_b", [P, P], BF)
        ones_f = sb(base, "ones_f", [P, P])
        causal = sb(base, "causal", [P, 2 * P])
        iota_p = sb(base, "iota_p", [P, P])
        iota_e = sb(base, "iota_e", [P, NT, NE])
        thresh = sb(base, "thresh", [P, NE, NT])
        iota_s = sb(base, "iota_s", [P, NSE, NE])
        tok_no = sb(base, "tok_no", [P, NT])
        ln1_sb = sb(base, "ln1_sb", [P, KC])
        ln2_sb = sb(base, "ln2_sb", [P, KC])
        decay_sb = sb(base, "decay_sb", [P, KC])
        bonus_sb = sb(base, "bonus_sb", [P, KC])
        ids_sb = sb(base, "ids_sb", [P, NT], I32)
        ids_f = sb(base, "ids_f", [P, NT])
        ge = sb(base, "ge", [P, 3, NT])
        emask = sb(base, "emask", [P, NE_A, NT])
        neghalf = sb(base, "neghalf", [P, 1])
        stat6 = sb(base, "stat6", [P, 2, 6])
        mv = sb(base, "mv", [P, 5, NT, 2])
        rs = sb(base, "rs", [P, 5, NT])
        rs_tmp = sb(base, "rs_tmp", [P, 5, NT, 3])
        rs_qkv = sb(base, "rs_qkv", [P, NT])
        logit = sb(base, "logit", [P, NT, NE])
        top8 = sb(base, "top8", [P, NT, 8])
        top8i = sb(base, "top8i", [P, NT, 8], U32)
        gate = sb(base, "gate", [P, 4, NT])
        sel_f = sb(base, "sel_f", [P, 2, NT])
        onehot = sb(base, "onehot", [P, 2, NT, NE])
        picked = sb(base, "picked", [P, NT + 1, NE], BF)
        nslot = sb(base, "nslot", [P, NE])
        cmp_e = sb(base, "cmp_e", [P, NE, NT])
        incl = sb(base, "incl", [P, NE])
        rowbase = sb(base, "rowbase", [P, NE])
        zero8 = sb(base, "zero8", [P, NE])
        rank = sb(base, "rank", [P, NT, NE])
        rank2 = sb(base, "rank2", [P, 2, NT, NE])
        pos_f = sb(base, "pos_f", [P, 2, NT])
        pos_i = sb(base, "pos_i", [P, 2, NT], I32)
        pos_si = sb(base, "pos_si", [P, 2, 2, NT], I32)
        pos_sf = sb(base, "pos_sf", [P, 2, 2, NT])
        cmp_s = sb(base, "cmp_s", [P, NSE, NE])
        slot_ef = sb(base, "slot_ef", [P, NSE])
        slot_e = sb(base, "slot_e", [P, NSE], I32)
        slot_tok = sb(base, "slot_tok", [P, NSE], I32)
        wabs = sb(base, "wabs", [P, 2])
        wmean = sb(base, "wmean", [P, 2])
        wscale = sb(base, "wscale", [P, 2])

        scope_w = ExitStack()
        we_sb = sb(scope_w, "we_sb", [P, NE * WE])
        RAW = (NE - 2) * WE
        w1_raw = we_sb[:, RAW:RAW + KC * F1]
        w2_raw = we_sb[:, RAW + KC * F1:RAW + KC * F1 + FC * D]

        scope_a = ExitStack()
        ctx_hi = sb(scope_a, "ctx_hi", [P, KC, NE_A * D], R)
        ctx_lo = sb(scope_a, "ctx_lo", [P, KC, NE_A * D], R)
        a_h = sb(scope_a, "a_h", [P, 2, D])
        a_hi = sb(scope_a, "a_hi", [P, 2, KC, P], R)
        a_lo = sb(scope_a, "a_lo", [P, 2, KC, P], R)
        a_u = sb(scope_a, "a_u", [P, 2, D])
        a_sig = sb(scope_a, "a_sig", [P, 2, D])
        a_act = sb(scope_a, "a_act", [P, 2, D])
        a_acthi = sb(scope_a, "a_acthi", [P, 2, KC, P], R)
        a_actlo = sb(scope_a, "a_actlo", [P, 2, KC, P], R)
        w_tmp = sb(scope_a, "w_tmp", [P, KC * F1])
        scope_a.close()

        scope_b = ExitStack()
        q_pack = [sb(scope_b, f"q_pack{i}", [P, H // 2, S], R) for i in range(2)]
        k_pack = [sb(scope_b, f"k_pack{i}", [P, H // 2, S], R) for i in range(2)]
        E_sb = sb(scope_b, "E_sb", [P, 3, 3 * P])
        v_aug = sb(scope_b, "v_aug", [P, 2, TB, H, 2 * HD])
        junk = sb(scope_b, "junk", [P, 2, 3 * P], BF)
        negmax = sb(scope_b, "negmax", [P, 2, TB, H])
        negmax_t = sb(scope_b, "negmax_t", [H, S], R)
        rden = sb(scope_b, "rden", [P, 2, H])
        scope_q = ExitStack()
        qk_parts = sb(scope_q, "qk_parts", [P, 2, 2, KC, S], R)
        xn_b = sb(scope_q, "xn_b", [P, 2, D])
        scope_q.close()
        scope_e = ExitStack()
        o_t = sb(scope_e, "o_t", [P, H // 4, S])
        h_tok = sb(scope_e, "h_tok", [P, 2, D])
        ho_t = sb(scope_e, "ho_t", [P, 2, KC, P])
        x2_n = sb(scope_e, "x2_n", [P, 2, D])
        x2_t = sb(scope_e, "x2_t", [P, 2, KC, P])
        scope_e.close()
        scope_b.close()

        scope_m = ExitStack()
        slot_oh = sb(scope_m, "slot_oh", [P, 4, P], R)
        slot_val = sb(scope_m, "slot_val", [P, 4, NSE], R)
        xg = sb(scope_m, "xg", [P, 2, D])
        xg_t = sb(scope_m, "xg_t", [P, 2, KC, P])
        sil = sb(scope_m, "sil", [P, 2, INTER])
        act_m = sb(scope_m, "act_m", [P, 2, INTER])
        act_t = sb(scope_m, "act_t", [P, 2, IC, P])
        y_sb = sb(scope_m, "y_sb", [P, 2, D])
        yc = sb(scope_m, "yc", [P, 2, 2, D])
        hc = sb(scope_m, "hc", [P, 2, D])
        scope_m.close()
        scope_w.close()

        scope_c = ExitStack()
        HB = B // 2
        o_st = sb(scope_c, "o_st", [P, KC, HB, S + 1])
        p_st = sb(scope_c, "p_st", [P, KC, HB, S + 1])
        q_st = sb(scope_c, "q_st", [P, KC, HB, S + 1])
        d_ou = sb(scope_c, "d_ou", [P, KC, HB, S])
        e_a = sb(scope_c, "e_a", [P, KC, HB, S])
        e_e = sb(scope_c, "e_e", [P, KC, HB, S])
        d_ok = sb(scope_c, "d_ok", [P, KC, HB, S])
        e_a2 = sb(scope_c, "e_a2", [P, KC, HB, S])
        e_e2 = sb(scope_c, "e_e2", [P, KC, HB, S])
        e_e2v = sb(scope_c, "e_e2v", [P, KC, HB, S])
        e_ev = sb(scope_c, "e_ev", [P, KC, HB, S])
        wkv_t = sb(scope_c, "wkv_t", [P, KC, HB, S])
        q_h = sb(scope_c, "q_h", [P, 2, D])
        q_r = sb(scope_c, "q_r", [P, 2, D])
        q_hb = sb(scope_c, "q_hb", [P, 2, D], BF)
        q_ht = sb(scope_c, "q_ht", [P, 2, KC, P], BF)
        q_g = sb(scope_c, "q_g", [P, 2, F1])
        q_gb = sb(scope_c, "q_gb", [P, 2, F1], BF)
        q_gt = sb(scope_c, "q_gt", [P, 2, FC, P], BF)
        q_s = sb(scope_c, "q_s", [P, 2, NT, 4])
        x_out = sb(scope_c, "x_out", [P, 2, D])
        scope_c.close()

        bank = [ctx.enter_context(nc.psum_tensor(f"bank{i}", [P, 512], F)) for i in range(8)]

        qk_dram = nc.dram_tensor("qk_dram", (B, 2, 2, D, S), F, kind="Internal").ap()
        xn_dram = nc.dram_tensor("xn_dram", (N, D), F, kind="Internal").ap()
        y_dram = nc.dram_tensor("y_dram", (NSLOT * P, D), F, kind="Internal").ap()

        in_x = sem("in_x")
        in_small = sem("in_small")
        in_ctx = sem("in_ctx")
        in_attn_w = sem("in_attn_w")
        in_ffn_w = sem("in_ffn_w")
        in_experts = sem("in_experts")
        consts = sem("consts")
        pool_chain = sem("pool_chain")
        dve_chain = sem("dve_chain")
        act_chain = sem("act_chain")
        stats_in = [sem(f"stats_in{i}") for i in range(5)]
        rstd_in = [sem(f"rstd_in{i}") for i in range(5)]
        ctx_hi_in = sem("ctx_hi_in")
        ctx_lo_in = sem("ctx_lo_in")
        w_abs_in = sem("w_abs_in")
        w_tot = sem("w_tot")
        w_scale_in = sem("w_scale_in")
        w_quant = sem("w_quant")
        wqkv_scaled = sem("wqkv_scaled")
        a_h_in = sem("a_h_in")
        a_tr = sem("a_tr")
        a_hi_in = sem("a_hi_in")
        a_lo_in = sem("a_lo_in")
        a_up = sem("a_up")
        a_u_in = sem("a_u_in")
        a_sig_in = sem("a_sig_in")
        a_act_in = sem("a_act_in")
        a_tr2 = sem("a_tr2")
        a_hi2_in = sem("a_hi2_in")
        a_lo2_in = sem("a_lo2_in")
        a_down = sem("a_down")
        x1_in = sem("x1_in")
        b_xn = sem("b_xn")
        b_tr = sem("b_tr")
        b_ht = sem("b_ht")
        b_qk = sem("b_qk")
        b_hi = sem("b_hi")
        b_lo = sem("b_lo")
        parts_out = [sem(f"parts_out{b}") for b in range(B)]
        pack_in = [sem(f"pack_in{b}") for b in range(B)]
        pack_ones = sem("pack_ones")
        b_v = sem("b_v")
        b_vaug = sem("b_vaug")
        s_done = sem("s_done")
        max_done = sem("max_done")
        nm_tr = sem("nm_tr")
        nm_row = sem("nm_row")
        nm_in = [sem(f"nm_in{b}") for b in range(B)]
        st_done = sem("st_done")
        exp_done = sem("exp_done")
        mask_done = sem("mask_done")
        av_done = sem("av_done")
        o_copied = sem("o_copied")
        ep_ot = sem("ep_ot")
        ep_h = sem("ep_h")
        ep_ht = sem("ep_ht")
        ep_htc = sem("ep_htc")
        ep_wo = sem("ep_wo")
        ep_x2 = sem("ep_x2")
        ep_xn = sem("ep_xn")
        ep_xt = sem("ep_xt")
        ep_xtc = sem("ep_xtc")
        ep_lg = sem("ep_lg")
        ep_lgc = sem("ep_lgc")
        x12_in = sem("x12_in")
        xn_out = [sem(f"xn_out{i}") for i in range(2)]
        gate_d = sem("gate_d")
        gate_e = sem("gate_e")
        picked_in = sem("picked_in")
        ranks = sem("ranks")
        route_oh = sem("route_oh")
        route_mm = sem("route_mm")
        route_tok = sem("route_tok")
        route_pos = sem("route_pos")
        xg_in = [sem(f"xg_in{i}") for i in range(2)]
        m_tr = sem("m_tr")
        m_xt = sem("m_xt")
        m_gu = sem("m_gu")
        m_sil = sem("m_sil")
        m_act = sem("m_act")
        m_at = sem("m_at")
        m_atc = sem("m_atc")
        m_y = sem("m_y")
        m_yc = sem("m_yc")
        y_out = [sem(f"y_out{i}") for i in range(2)]
        yc_in = [sem(f"yc_in{i}") for i in range(2)]
        x3_in = sem("x3_in")
        c_h = sem("c_h")
        c_tr = sem("c_tr")
        c_kt = sem("c_kt")
        c_dou = sem("c_dou")
        c_ea = sem("c_ea")
        c_dok = sem("c_dok")
        c_ea2 = sem("c_ea2")
        c_ev = sem("c_ev")
        c_y = sem("c_y")
        c_ytr = sem("c_ytr")
        x4_in = sem("x4_in")
        d_hb = sem("d_hb")
        d_htr = sem("d_htr")
        d_htc = sem("d_htc")
        d_up = sem("d_up")
        d_gelu = sem("d_gelu")
        d_gb = sem("d_gb")
        d_gtr = sem("d_gtr")
        d_gtc = sem("d_gtc")
        d_down = sem("d_down")
        d_out = sem("d_out")
        out_done = [sem(f"out_done{i}") for i in range(2)]

        block = ctx.enter_context(nc.Block())

        NSTEP = B * H
        S_FIRST = 6
        NM_STEP = S_FIRST + H // 2
        V_STEP = 13
        EP_OT = [0, 2]
        EP_HT = [3, 6]
        EP_WO = [4, 7]
        EP_XT = [8, 11]
        EP_LG = [9, 12]

        def where(n):
            return n // H, n % H

        @block.sync
        def _(sp):
            xv = x.rearrange("(i p) d -> p i d", p=P)
            sp.dma_start(x_sb[:, 0:2, :], xv[:, 0:2, :]).then_inc(in_x, 16)
            sp.dma_start(ctx_sb[:, :, :], ctx_t.rearrange("(k p) e f -> p k (e f)", p=P)).then_inc(in_ctx, 16)
            sp.dma_start(ids_sb[:, :], ids).then_inc(in_small, 16)
            sp.dma_start(x_sb[:, 2:NT, :], xv[:, 2:NT, :]).then_inc(in_x, 16)
            for dst, src in ((ln1_sb, ln1), (ln2_sb, ln2), (decay_sb, decay), (bonus_sb, bonus)):
                sp.dma_start(dst[:, :], src).then_inc(in_small, 16)
            sp.dma_start(wqkv[:, :, :], wqkv_t.rearrange("(k p) n -> p k n", p=P)).then_inc(in_attn_w, 16)
            sp.dma_start(wo[:, :, :], wo_t.rearrange("(k p) n -> p k n", p=P)).then_inc(in_attn_w, 16)
            sp.dma_start(wr[:, :, :], wr_t.rearrange("(k p) n -> p k n", p=P)).then_inc(in_attn_w, 16)
            sp.dma_start(w1_raw.rearrange("p (k n) -> p k n", k=KC), w1_t.rearrange("k p n -> p k n")).then_inc(in_ffn_w, 16)
            sp.dma_start(w2_raw.rearrange("p (k n) -> p k n", k=FC), w2_t.rearrange("k p n -> p k n")).then_inc(in_ffn_w, 16)
            for e in range(NE - 2):
                sp.dma_start(we_sb[:, e * WE:(e + 1) * WE], wexp[e]).then_inc(in_experts, 16)
            sp.wait_ge(w_quant, 1)
            for e in range(NE - 2, NE):
                sp.dma_start(we_sb[:, e * WE:(e + 1) * WE], wexp[e]).then_inc(in_experts, 16)

            def load_pack(b):
                sp.wait_ge(parts_out[b], 32)
                if b >= 2:
                    sp.wait_ge(st_done, H * (b - 1))
                else:
                    sp.wait_ge(pack_ones, 2)
                for qk, pack, order in ((0, q_pack, (0, 1, 0)), (1, k_pack, (0, 0, 1))):
                    for odd in range(2):
                        for c, part in enumerate(order):
                            r0 = 64 * odd + HD * c
                            src = qk_dram[b, qk, part].rearrange("(j o d) n -> o d j n", o=2, d=HD)[odd]
                            sp.dma_start(pack[b % 2][r0:r0 + HD, :, :].bitcast(F), src).then_inc(pack_in[b], 16)

            def store_parts(b):
                for qk in range(2):
                    sp.wait_ge(b_lo, 2 * b + qk + 1)
                    sp.dma_start(qk_dram[b, qk].rearrange("l (k p) n -> p l k n", p=P),
                                 qk_parts[:, qk, :, :, :].bitcast(F)).then_inc(parts_out[b], 16)

            def store_max(b):
                sp.wait_ge(nm_row, b + 1)
                for odd in range(2):
                    r0 = 64 * odd + 3 * HD
                    sp.dma_start(q_pack[b % 2][r0:r0 + 1, :, :].bitcast(F), negmax_t[odd:H:2, :].bitcast(F)).then_inc(nm_in[b], 16)

            store_parts(0)
            store_parts(1)
            load_pack(0)
            store_parts(2)
            load_pack(1)
            store_parts(3)
            for b in range(B + 1):
                if b < B:
                    store_max(b)
                if 1 <= b < B - 1:
                    load_pack(b + 1)
                for i in range((b - 1) * TB, b * TB):
                    if i >= 0:
                        sp.wait_ge(ep_xn, i + 1)
                        sp.dma_start(xn_dram[i * P:(i + 1) * P, :], x2_n[:, i % 2, :]).then_inc(xn_out[i % 2], 16)

            def store_slot(s, u):
                sp.wait_ge(m_yc, s + 1)
                sp.dma_start(y_dram[bass.ds(s * P, P), :], y_sb[:, u, :]).then_inc(y_out[u], 16)

            with sp.Fori(0, NSLOT // 2) as i:
                for u in range(2):
                    store_slot(i * 2 + u, u)
            for s in range(NSLOT - NSLOT % 2, NSLOT):
                store_slot(s, s % 2)

            for i in range(NT):
                sp.wait_ge(d_out, i + 1)
                sp.dma_start(out[i * P:(i + 1) * P, :], x_out[:, i % 2, :]).then_inc(out_done[i % 2], 16)
            for u in range(2):
                sp.wait_ge(out_done[u], 16 * (NT // 2))

        @block.gpsimd
        def _(pool):
            g = nc.gpsimd
            chain = [0]

            def link(ins):
                chain[0] += 1
                ins.then_inc(pool_chain, 1)
                pool.wait_ge(pool_chain, chain[0])

            def rsqrt(kind, i):
                pool.wait_ge(stats_in[kind], i + 1)
                link(g.tensor_scalar(rs_tmp[:, kind, i, 0:1], mv[:, kind, i, 1:2], EPS, 1.0, ALU.add, ALU.mult))
                return g.tensor_tensor(rs[:, kind, i:i + 1], rs_tmp[:, kind, i, 0:1], neghalf[:, :], ALU.pow)

            link(g.memset(neghalf[:, :], -0.5))
            g.memset(ones_f[:, :], 1.0)
            g.memset(ones_b[:, :], 1.0)
            g.memset(earlier[:, :], 1.0)
            g.memset(ident_b[:, :], 0.0)
            g.memset(causal[:, :], 0.0)
            g.memset(picked[:, :, :], 0.0)
            g.memset(zero8[:, :], 0.0)
            link(g.memset(ident[:, :], 0.0))
            link(g.affine_select(out=ident[:, :], in_=ident[:, :], compare_op=ALU.not_equal, fill=1.0,
                                 base=0, pattern=[[-1, P]], channel_multiplier=1))
            for i in range(NT):
                rsqrt(0, i).then_inc(rstd_in[0], 1)
            g.iota(iota_p[:, :], pattern=[[1, P]], base=0, channel_multiplier=0,
                   allow_small_or_imprecise_dtypes=True)
            g.iota(iota_e[:, :, :], pattern=[[0, NT], [1, NE]], base=0, channel_multiplier=0,
                   allow_small_or_imprecise_dtypes=True)
            g.iota(thresh[:, :, :], pattern=[[0, NE], [P, NT]], base=0, channel_multiplier=0,
                   allow_small_or_imprecise_dtypes=True)
            g.iota(iota_s[:, :, :], pattern=[[1, NSE], [0, NE]], base=0, channel_multiplier=0,
                   allow_small_or_imprecise_dtypes=True)
            g.iota(tok_no[:, :], pattern=[[P, NT]], base=0, channel_multiplier=1,
                   allow_small_or_imprecise_dtypes=True)
            g.affine_select(out=ident_b[:, :], in_=ident_b[:, :], compare_op=ALU.not_equal, fill=1.0,
                            base=0, pattern=[[-1, P]], channel_multiplier=1)
            g.affine_select(out=earlier[:, :], in_=earlier[:, :], compare_op=ALU.is_gt, fill=0.0,
                            base=0, pattern=[[1, P]], channel_multiplier=-1)
            link(g.affine_select(out=causal[:, P:2 * P], in_=causal[:, P:2 * P], compare_op=ALU.is_ge,
                                 fill=-BIG, base=0, pattern=[[-1, P]], channel_multiplier=1))
            pool.sem_inc(consts, 1)

            pool.wait_ge(w_scale_in, 1)
            for j, (raw, dst) in enumerate(((w1_raw, w1q[:, :, :].rearrange("p k n -> p (k n)")),
                                            (w2_raw, w2q[:, :, :].rearrange("p k n -> p (k n)")))):
                link(g.tensor_scalar(w_tmp[:, :], raw, wscale[:, j:j + 1], MAGIC, ALU.mult, ALU.add))
                link(g.tensor_scalar(w_tmp[:, :], w_tmp[:, :], MAGIC + 1.0, MAGIC - 1.0, ALU.min, ALU.max))
                last = g.tensor_scalar(dst, w_tmp[:, :], -MAGIC, 1.0, ALU.add, ALU.mult)
                if j == 0:
                    link(last)
            last.then_inc(w_quant, 1)

            for i in range(NT):
                link(rsqrt(1, i))
                link(g.tensor_tensor(rs_tmp[:, 1, i, 1:2], rs[:, 1, i:i + 1], rs[:, 1, i:i + 1], ALU.mult))
                link(g.tensor_tensor(rs_tmp[:, 1, i, 1:2], rs_tmp[:, 1, i, 1:2], mv[:, 1, i, 1:2], ALU.mult))
                link(g.tensor_scalar(rs_tmp[:, 1, i, 1:2], rs_tmp[:, 1, i, 1:2], EPS, 1.0, ALU.add, ALU.mult))
                link(g.tensor_tensor(rs_tmp[:, 1, i, 2:3], rs_tmp[:, 1, i, 1:2], neghalf[:, :], ALU.pow))
                g.tensor_tensor(rs_qkv[:, i:i + 1], rs[:, 1, i:i + 1], rs_tmp[:, 1, i, 2:3], ALU.mult)\
                    .then_inc(rstd_in[1], 1)

            pool.wait_ge(a_down, NT)
            pool.wait_ge(x1_in, NT)
            pool.wait_ge(w_quant, 1)
            for i in range(2):
                g.memset(k_pack[i][:, :, :].bitcast(F), 1.0).then_inc(pack_ones, 1)
            for i in range(2):
                g.memset(v_aug[:, i, :, :, :], 1.0).then_inc(pack_ones, 1)

            for n in range(NSTEP + H):
                b, h = where(n)
                if n < NSTEP:
                    pool.wait_ge(exp_done, n + 1)
                    diag = E_sb[:, n % 3, :]
                    g.affine_select(out=diag[:, 0:P], in_=diag[:, 0:P], compare_op=ALU.is_ge, fill=0.0,
                                    base=0, pattern=[[1, P]], channel_multiplier=-1)
                    g.affine_select(out=diag[:, 2 * P:3 * P], in_=diag[:, 2 * P:3 * P], compare_op=ALU.is_ge,
                                    fill=0.0, base=0, pattern=[[1, P]], channel_multiplier=-1)\
                        .then_inc(mask_done, 1)
                if b >= 1:
                    for t in range(TB):
                        if h == EP_WO[t] + 1:
                            i = (b - 1) * TB + t
                            pool.wait_ge(stats_in[2], i + 1)
                            link(g.tensor_tensor(rs_tmp[:, 2, i, 1:2], mv[:, 2, i, 0:1], mv[:, 2, i, 0:1], ALU.mult))
                            link(g.tensor_tensor(rs_tmp[:, 2, i, 1:2], rs_tmp[:, 2, i, 1:2], mv[:, 2, i, 1:2], ALU.add))
                            link(g.tensor_scalar(rs_tmp[:, 2, i, 1:2], rs_tmp[:, 2, i, 1:2], EPS, 1.0, ALU.add, ALU.mult))
                            g.tensor_tensor(rs[:, 2, i:i + 1], rs_tmp[:, 2, i, 1:2], neghalf[:, :], ALU.pow)\
                                .then_inc(rstd_in[2], 1)
                            pool.wait_ge(ep_x2, i + 1)
                            g.tensor_tensor(x_sb[:, i, :], x_sb[:, i, :], res[:, i, :], ALU.add).then_inc(x12_in, 1)

            pool.wait_ge(route_tok, 1)
            for u in range(2):
                pool.wait_ge(xn_out[u], 16 * (NT // 2))
            for s in range(NSLOT):
                if s >= 2:
                    pool.wait_ge(m_tr, s - 1)
                g.indirect_dma_start(xg[:, s % 2, :], None, xn_dram,
                                     bass.IndirectOffsetOnAxis(slot_tok[:, s:s + 1], 0)).then_inc(xg_in[s % 2], 16)
            for u in range(2):
                pool.wait_ge(y_out[u], 16 * ((NSLOT + 1 - u) // 2))
            pool.wait_ge(route_pos, 1)

            def gather(i):
                if i >= 2:
                    pool.wait_ge(x3_in, i - 1)
                for c in range(2):
                    g.indirect_dma_start(yc[:, i % 2, c, :], None, y_dram,
                                         bass.IndirectOffsetOnAxis(pos_i[:, c, i:i + 1], 0))\
                        .then_inc(yc_in[i % 2], 16)

            gather(0)
            gather(1)
            for i in range(NT):
                rsqrt(3, i).then_inc(rstd_in[3], 1)
                if i + 2 < NT:
                    gather(i + 2)

            for half in range(2):
                for k in range(KC):
                    n = half * KC + k
                    v = ctx_sb[:, k, half * HB * S:(half + 1) * HB * S].rearrange("p (b t) -> p b t", b=HB)
                    pool.wait_ge(c_ea2, n + 1)
                    pool.wait_ge(c_ea, n + 1)
                    if n >= KC:
                        pool.wait_ge(c_y, n - KC + 1)
                    g.tensor_tensor(e_e2v[:, k, :, :], e_e2[:, k, :, :], v, ALU.mult).then_inc(c_ev, 1)
                    g.tensor_tensor(e_ev[:, k, :, :], e_e[:, k, :, :], v, ALU.mult).then_inc(c_ev, 1)
            for i in range(NT):
                rsqrt(4, i).then_inc(rstd_in[4], 1)

        @block.scalar
        def _(act):
            a = nc.scalar
            act.wait_ge(in_ctx, 16)
            for k in range(KC):
                a.activation(ctx_hi[:, k, :], ctx_sb[:, k, :], ACT.Copy).then_inc(ctx_hi_in, 1)

            def a_first(i):
                act.wait_ge(a_tr, i + 1)
                if i >= 2:
                    act.wait_ge(a_up, i - 1)
                a.activation(a_hi[:, i % 2, :, :].rearrange("p k n -> p (k n)"), bank[4][:, 0:D],
                             ACT.Copy).then_inc(a_hi_in, 1)

            a_first(0)
            for i in range(NT):
                if i + 1 < NT:
                    a_first(i + 1)
                act.wait_ge(a_u_in, i + 1)
                a.activation(a_sig[:, i % 2, :], a_u[:, i % 2, :], ACT.Silu).then_inc(a_sig_in, 1)
                act.wait_ge(a_tr2, i + 1)
                if i >= 2:
                    act.wait_ge(a_down, i - 1)
                a.activation(a_acthi[:, i % 2, :, :].rearrange("p k n -> p (k n)"), bank[5][:, 0:D],
                             ACT.Copy).then_inc(a_hi2_in, 1)

            for b in range(B):
                for t in range(TB):
                    i = b * TB + t
                    act.wait_ge(b_tr, i + 1)
                    a.activation(h_t[:, :, i * P:(i + 1) * P], bank[6][:, 0:D].rearrange("p (k n) -> p k n", k=KC),
                                 ACT.Copy).then_inc(b_ht, 1)
                for qk in range(2):
                    act.wait_ge(b_qk, 2 * b + qk + 1)
                    if b >= 1:
                        act.wait_ge(parts_out[b - 1], 32)
                    elif qk == 0:
                        act.wait_ge(a_down, NT)
                    a.activation(qk_parts[:, qk, 0, :, :], bank[7 if qk == 0 else 0][:, :].rearrange("p (k n) -> p k n", k=KC),
                                 ACT.Copy, scale=(HD ** -0.5 if qk == 0 else 1.0)).then_inc(b_hi, 1)

            def v_copy(b):
                act.wait_ge(b_v, b + 1)
                if b < 2:
                    act.wait_ge(pack_ones, 4)
                a.activation(v_aug[:, b % 2, :, :, 0:HD],
                             bank[1][:, :].rearrange("p (t h d) -> p t h d", t=TB, h=H), ACT.Copy).then_inc(b_vaug, 1)

            def nm_copy(b):
                act.wait_ge(nm_tr, b + 1)
                if b >= 1:
                    act.wait_ge(nm_in[b - 1], 32)
                a.activation(negmax_t[:, :], bank[1][0:H, 0:S], ACT.Copy, scale=-1.0).then_inc(nm_row, 1)

            v_copy(0)
            nm_copy(0)
            act.wait_ge(parts_out[B - 1], 32)
            for n in range(NSTEP + H):
                b, h = where(n)
                if n < NSTEP:
                    act.wait_ge(st_done, n + 1)
                    if n >= 3:
                        act.wait_ge(av_done, n - 2)
                    a.activation(E_sb[:, n % 3, :], bank[4 + n % 3][:, 0:3 * P], ACT.Exp).then_inc(exp_done, 1)
                if n >= 1 and n <= NSTEP and n % 4 == 0:
                    gidx = n // 4 - 1
                    act.wait_ge(av_done, n)
                    if gidx >= 4:
                        act.wait_ge(ep_ot, TB * (gidx // 4))
                    a.activation(o_t[:, gidx % 4, :], bank[7][:, 0:S], ACT.Copy).then_inc(o_copied, 1)
                if n < NSTEP and b + 1 < B:
                    if h == V_STEP:
                        v_copy(b + 1)
                    if h == NM_STEP:
                        nm_copy(b + 1)
                if b >= 1:
                    for t in range(TB):
                        i = (b - 1) * TB + t
                        if h == EP_HT[t]:
                            act.wait_ge(ep_ht, i + 1)
                            a.activation(ho_t[:, t, :, :], bank[1][:, 0:D].rearrange("p (k n) -> p k n", k=KC),
                                         ACT.Copy).then_inc(ep_htc, 1)
                        if h == EP_XT[t]:
                            act.wait_ge(ep_xt, i + 1)
                            for k in range(KC):
                                last = a.activation(x2_t[:, t, k, :], bank[0][:, k * P:(k + 1) * P], ACT.Copy,
                                                    scale=ln2_sb[:, k:k + 1])
                            last.then_inc(ep_xtc, 1)
            act.wait_ge(gate_d, 1)
            a.activation(gate[:, 1, :], gate[:, 0, :], ACT.Exp).then_inc(gate_e, 1)

            def x_copy(s, u):
                act.wait_ge(m_tr, s + 1)
                for k in range(KC):
                    last = a.activation(xg_t[:, u, k, :], bank[0][:, k * P:(k + 1) * P], ACT.Copy,
                                        scale=ln2_sb[:, k:k + 1])
                last.then_inc(m_xt, 1)

            def silu(s, u):
                act.wait_ge(m_gu, s + 1)
                a.activation(sil[:, u, :], bank[1 + u][:, :], ACT.Silu).then_inc(m_sil, 1)

            def y_copy(s, u, first=False):
                act.wait_ge(m_y, s + 1)
                if not first:
                    act.wait_ge(y_out[u], (s - u) * 8)
                a.activation(y_sb[:, u, :], bank[6 + u][:, 0:D], ACT.Copy).then_inc(m_yc, 1)

            x_copy(0, 0)
            x_copy(1, 1)
            silu(0, 0)
            for s in range(2):
                silu(s + 1, (s + 1) % 2)
                x_copy(s + 2, s % 2)
                y_copy(s, s % 2, first=True)
            with act.Fori(1, (NSLOT - 3) // 2) as i:
                for u in range(2):
                    s = i * 2 + u
                    silu(s + 1, 1 - u)
                    x_copy(s + 2, u)
                    y_copy(s, u)
            for s in range((NSLOT - 3) // 2 * 2, NSLOT):
                if s + 1 < NSLOT:
                    silu(s + 1, (s + 1) % 2)
                if s + 2 < NSLOT:
                    x_copy(s + 2, s % 2)
                y_copy(s, s % 2)

            for i in range(NT):
                act.wait_ge(c_tr, i + 1)
                a.activation(h_t[:, :, i * P:(i + 1) * P], bank[i % 2][:, 0:D].rearrange("p (k n) -> p k n", k=KC),
                             ACT.Copy).then_inc(c_kt, 1)
                if i % (NT // 2) == NT // 2 - 1:
                    half = i // (NT // 2)
                    for k in range(KC):
                        n = half * KC + k
                        act.wait_ge(c_dok, 2 * n + 2)
                        a.activation(e_a2[:, k, :, :], e_a2[:, k, :, :], ACT.Exp)
                        a.activation(e_e2[:, k, :, :], e_e2[:, k, :, :], ACT.Exp).then_inc(c_ea2, 1)
                        act.wait_ge(c_dou, 2 * n + 2)
                        a.activation(e_a[:, k, :, :], e_a[:, k, :, :], ACT.Exp)
                        a.activation(e_e[:, k, :, :], e_e[:, k, :, :], ACT.Exp).then_inc(c_ea, 1)

            for i in range(NT):
                act.wait_ge(d_up, i + 1)
                if i >= 2:
                    act.wait_ge(d_gb, i - 1)
                for c in range(2):
                    last = a.activation(q_g[:, i % 2, c * 512:(c + 1) * 512], bank[2 + c][:, :], ACT.Gelu,
                                        scale=q_s[:, 0, i, 2:3])
                last.then_inc(d_gelu, 1)
                act.wait_ge(d_gtr, i + 1)
                if i >= 2:
                    act.wait_ge(d_down, i - 1)
                a.activation(q_gt[:, i % 2, :, :].rearrange("p k n -> p (k n)"), bank[4][:, :].bitcast(BF),
                             ACT.Copy).then_inc(d_gtc, 1)

        @block.vector
        def _(dve):
            v = nc.vector
            chain = [0]

            def link(ins):
                chain[0] += 1
                ins.then_inc(dve_chain, 1)
                dve.wait_ge(dve_chain, chain[0])

            def stats(kind, i, src):
                link(v.bn_stats(stat6[:, i % 2, :], src))
                v.bn_aggr(mv[:, kind, i, :], stat6[:, i % 2, :]).then_inc(stats_in[kind], 1)

            def normalise(dst, kind, i, src, factor=None):
                return v.tensor_scalar(dst, src, mv[:, kind, i, 0:1],
                                       rs[:, kind, i:i + 1] if factor is None else factor,
                                       ALU.subtract, ALU.mult)

            dve.wait_ge(in_x, 32)
            for i in range(2):
                stats(0, i, x_sb[:, i, :])
            dve.wait_ge(in_ctx, 16)
            for k in range(KC):
                dve.wait_ge(ctx_hi_in, k + 1)
                v.tensor_tensor(ctx_lo[:, k, :], ctx_sb[:, k, :], ctx_hi[:, k, :].bitcast(F), ALU.subtract)\
                    .then_inc(ctx_lo_in, 1)
            dve.wait_ge(in_small, 80)
            link(v.tensor_copy(ids_f[:, :], ids_sb[:, :]))
            for j in range(3):
                last = v.tensor_scalar(ge[:, j, :], ids_f[:, :], float(3125 * (j + 1)), None, ALU.is_ge)
            link(last)
            v.tensor_scalar(emask[:, 0, :], ge[:, 0, :], -1.0, 1.0, ALU.mult, ALU.add)
            v.tensor_tensor(emask[:, 1, :], ge[:, 0, :], ge[:, 1, :], ALU.subtract)
            v.tensor_tensor(emask[:, 2, :], ge[:, 1, :], ge[:, 2, :], ALU.subtract)
            link(v.tensor_copy(emask[:, 3, :], ge[:, 2, :]))
            for i in range(2, NT):
                stats(0, i, x_sb[:, i, :])

            def a_norm(i):
                dve.wait_ge(rstd_in[0], i + 1)
                if i >= 2:
                    dve.wait_ge(a_tr, i - 1)
                normalise(a_h[:, i % 2, :], 0, i, x_sb[:, i, :]).then_inc(a_h_in, 1)

            def a_low(i):
                dve.wait_ge(a_hi_in, i + 1)
                v.tensor_tensor(a_lo[:, i % 2, :, :].rearrange("p k n -> p (k n)"), bank[4][:, 0:D],
                                a_hi[:, i % 2, :, :].rearrange("p k n -> p (k n)").bitcast(F), ALU.subtract)\
                    .then_inc(a_lo_in, 1)

            def a_select(i):
                dve.wait_ge(a_up, i + 1)
                u = a_u[:, i % 2, :]
                link(v.tensor_scalar(u, bank[0][:, 0:D], emask[:, 0, i:i + 1], None, ALU.mult))
                for e in range(1, NE_A):
                    last = v.scalar_tensor_tensor(u, bank[e // 2][:, (e % 2) * D:(e % 2 + 1) * D],
                                                  emask[:, e, i:i + 1], u, ALU.mult, ALU.add)
                    if e < NE_A - 1:
                        link(last)
                last.then_inc(a_u_in, 1)

            def a_gate(i):
                dve.wait_ge(a_sig_in, i + 1)
                if i >= 2:
                    dve.wait_ge(a_tr2, i - 1)
                v.tensor_tensor(a_act[:, i % 2, :], a_sig[:, i % 2, :], a_u[:, i % 2, :], ALU.mult)\
                    .then_inc(a_act_in, 1)

            def a_low2(i):
                dve.wait_ge(a_hi2_in, i + 1)
                v.tensor_tensor(a_actlo[:, i % 2, :, :].rearrange("p k n -> p (k n)"), bank[5][:, 0:D],
                                a_acthi[:, i % 2, :, :].rearrange("p k n -> p (k n)").bitcast(F), ALU.subtract)\
                    .then_inc(a_lo2_in, 1)

            def a_add(i):
                dve.wait_ge(a_down, i + 1)
                for e in range(NE_A):
                    link(v.scalar_tensor_tensor(x_sb[:, i, :], bank[2 + e // 2][:, (e % 2) * D:(e % 2 + 1) * D],
                                                emask[:, e, i:i + 1], x_sb[:, i, :], ALU.mult, ALU.add))
                link(v.bn_stats(stat6[:, i % 2, :], x_sb[:, i, :]))
                v.bn_aggr(mv[:, 1, i, :], stat6[:, i % 2, :]).then_inc(stats_in[1], 1)

            dve.wait_ge(in_small, 80)
            a_norm(0)
            a_low(0)
            for i in range(NT):
                if i + 1 < NT:
                    a_norm(i + 1)
                a_select(i)
                if i + 1 < NT:
                    a_low(i + 1)
                a_gate(i)
                if i >= 1:
                    a_add(i - 1)
                a_low2(i)
                if i == 2:
                    dve.wait_ge(in_ffn_w, 32)
                    v.tensor_reduce(wabs[:, 0:1], w1_raw, AX, ALU.add, apply_absolute_value=True)
                    v.tensor_reduce(wabs[:, 1:2], w2_raw, AX, ALU.add, apply_absolute_value=True).then_inc(w_abs_in, 1)
                if i == 4:
                    dve.wait_ge(w_tot, 1)
                    link(v.tensor_scalar(wmean[:, :], bank[7][:, 0:2], 1.0 / (F1 * D), EPS, ALU.mult, ALU.max))
                    v.reciprocal(wscale[:, :], wmean[:, :]).then_inc(w_scale_in, 1)
                if i == 5:
                    dve.wait_ge(in_attn_w, 48)
                    for k in range(KC):
                        last = v.tensor_scalar(wqkv[:, k, :], wqkv[:, k, :], ln1_sb[:, k:k + 1], None, ALU.mult)
                    last.then_inc(wqkv_scaled, 1)
            a_add(NT - 1)

            for b in range(B):
                for t in range(TB):
                    i = b * TB + t
                    dve.wait_ge(rstd_in[1], i + 1)
                    last = normalise(res[:, i, :], 1, i, x_sb[:, i, :])
                    if i >= 2:
                        dve.wait_ge(b_tr, i - 1)
                    normalise(xn_b[:, i % 2, :], 1, i, x_sb[:, i, :], rs_qkv[:, i:i + 1]).then_inc(b_xn, 1)
                    if i == NT - 1:
                        last = None
                if b == 0:
                    v.tensor_copy(gate[:, 2, 0:1], ln1_sb[:, 0:1]).then_inc(x1_in, NT)
                for qk in range(2):
                    dve.wait_ge(b_hi, 2 * b + qk + 1)
                    lo = qk_parts[:, qk, 1, :, :]
                    ps = bank[7 if qk == 0 else 0][:, :].rearrange("p (k n) -> p k n", k=KC)
                    hi = qk_parts[:, qk, 0, :, :].bitcast(F)
                    v.scalar_tensor_tensor(lo, ps, HD ** -0.5 if qk == 0 else 1.0, hi, ALU.mult, ALU.subtract)\
                        .then_inc(b_lo, 1)

            def row_max(m):
                b, h = where(m)
                dve.wait_ge(s_done, m + 1)
                if h == 0 and b >= 2:
                    dve.wait_ge(nm_tr, b - 1)
                for t in range(TB):
                    keys = (t + 1) * P
                    last = v.tensor_tensor_reduce(
                        out=junk[:, m % 2, t * P:t * P + keys], in0=bank[2 + h % 2][:, t * P:t * P + keys],
                        in1=causal[:, 2 * P - keys:2 * P], scale=1.0, scalar=-3e38, op0=ALU.add, op1=ALU.max,
                        accum_out=negmax[:, b % 2, t, h:h + 1])
                last.then_inc(max_done, 1)

            def ep_norm(i):
                t = i % TB
                dve.wait_ge(ep_ot, i + 1)
                o = bank[0][:, :].rearrange("p (h c) -> p h c", h=H)
                link(v.reciprocal(rden[:, t, :], o[:, :, HD]))
                if i >= 2:
                    dve.wait_ge(ep_ht, i - 1)
                v.tensor_tensor(h_tok[:, t, :].rearrange("p (h d) -> p h d", h=H), o[:, :, 0:HD],
                                rden[:, t, :].unsqueeze(2).to_broadcast([P, H, HD]), ALU.mult).then_inc(ep_h, 1)

            def ep_add(i):
                dve.wait_ge(ep_wo, i + 1)
                link(v.tensor_tensor(res[:, i, :], bank[1][:, D:2 * D], res[:, i, :], ALU.add))
                link(v.bn_stats(stat6[:, i % 2, :], res[:, i, :]))
                v.bn_aggr(mv[:, 2, i, :], stat6[:, i % 2, :]).then_inc(stats_in[2], 1)
                v.tensor_copy(gate[:, 2, 0:1], ln1_sb[:, 0:1]).then_inc(ep_x2, 1)

            def ep_rms(i):
                dve.wait_ge(rstd_in[2], i + 1)
                if i >= 2:
                    dve.wait_ge(ep_xt, i - 1)
                    dve.wait_ge(xn_out[i % 2], 16 * (i // 2))
                v.tensor_scalar(x2_n[:, i % 2, :], res[:, i, :], rs[:, 2, i:i + 1], None, ALU.mult).then_inc(ep_xn, 1)

            def ep_top(i):
                dve.wait_ge(ep_lg, i + 1)
                link(v.tensor_copy(logit[:, i, :], bank[0][:, D:D + NE]))
                link(v.max(top8[:, i, :], logit[:, i, :]))
                v.max_index(top8i[:, i, :], top8[:, i, :], logit[:, i, :]).then_inc(ep_lgc, 1)

            for m in range(H):
                row_max(m)
            for n in range(NSTEP + H):
                b, h = where(n)
                if b >= 1:
                    for t in range(TB):
                        i = (b - 1) * TB + t
                        if h == EP_OT[t]:
                            ep_norm(i)
                        if h == EP_WO[t]:
                            ep_add(i)
                        if h == EP_WO[t] + 3:
                            ep_rms(i)
                        if h == EP_LG[t]:
                            ep_top(i)
                if n < NSTEP and b + 1 < B and S_FIRST <= h < S_FIRST + H // 2:
                    for j in range(2):
                        row_max((b + 1) * H + 2 * (h - S_FIRST) + j)

            dve.wait_ge(ep_lgc, NT)
            v.tensor_tensor(gate[:, 0, :], top8[:, :, 1], top8[:, :, 0], ALU.subtract).then_inc(gate_d, 1)
            for c in range(2):
                last = v.tensor_copy(sel_f[:, c, :], top8i[:, :, c])
            link(last)
            for c in range(2):
                last = v.tensor_tensor(onehot[:, c, :, :], iota_e[:, :, :],
                                       sel_f[:, c, :].unsqueeze(2).to_broadcast([P, NT, NE]), ALU.is_equal)
            link(last)
            v.tensor_tensor(picked[:, 0:NT, :], onehot[:, 0, :, :], onehot[:, 1, :, :], ALU.add).then_inc(picked_in, 1)
            dve.wait_ge(gate_e, 1)
            link(v.tensor_scalar(gate[:, 0, :], gate[:, 1, :], 1.0, None, ALU.add))
            link(v.reciprocal(gate[:, 2, :], gate[:, 0, :]))
            v.tensor_tensor(gate[:, 3, :], gate[:, 1, :], gate[:, 2, :], ALU.mult)
            dve.wait_ge(ranks, 1)
            counts = bank[1][:, NT * NE:(NT + 1) * NE]
            link(v.tensor_tensor(cmp_e[:, :, :], thresh[:, :, :], counts.unsqueeze(2).to_broadcast([P, NE, NT]),
                                 ALU.is_lt))
            link(v.tensor_reduce(nslot[:, :], cmp_e[:, :, :], AX, ALU.add))
            link(v.tensor_tensor_scan(incl[:, :], nslot[:, :], zero8[:, :], 0.0, ALU.add, ALU.add))
            link(v.tensor_tensor(rowbase[:, :], incl[:, :], nslot[:, :], ALU.subtract))
            link(v.scalar_tensor_tensor(rank[:, :, :], rowbase[:, :].unsqueeze(1).to_broadcast([P, NT, NE]), float(P),
                                        bank[1][:, 0:NT * NE].rearrange("p (i e) -> p i e", i=NT), ALU.mult, ALU.add))
            for c in range(2):
                last = v.tensor_tensor(rank2[:, c, :, :], onehot[:, c, :, :], rank[:, :, :], ALU.mult)
            link(last)
            link(v.tensor_reduce(pos_f[:, :, :], rank2[:, :, :, :], AX, ALU.add))
            link(v.tensor_copy(pos_i[:, :, :], pos_f[:, :, :]))
            v.tensor_scalar(pos_si[:, 0, :, :], pos_i[:, :, :], 7, None, ALU.arith_shift_right)
            link(v.tensor_scalar(pos_si[:, 1, :, :], pos_i[:, :, :], P - 1, None, ALU.bitwise_and))
            link(v.tensor_copy(pos_sf[:, :, :, :], pos_si[:, :, :, :]))
            for n in range(2 * NT):
                c, i = n // NT, n % NT
                if n >= 4:
                    dve.wait_ge(route_mm, n - 3)
                v.tensor_scalar(slot_oh[:, n % 4, :], iota_p[:, :], pos_sf[:, 1, c, i:i + 1], None, ALU.is_equal)
                v.tensor_scalar(slot_val[:, n % 4, :], iota_s[:, :, 0], pos_sf[:, 0, c, i:i + 1],
                                tok_no[:, i:i + 1], ALU.is_equal, ALU.mult).then_inc(route_oh, 1)
            link(v.tensor_tensor(cmp_s[:, :, :], iota_s[:, :, :], incl[:, :].unsqueeze(1).to_broadcast([P, NSE, NE]),
                                 ALU.is_ge))
            link(v.tensor_reduce(slot_ef[:, :], cmp_s[:, :, :], AX, ALU.add))
            v.tensor_scalar(slot_e[:, :], slot_ef[:, :], float(NE - 1), None, ALU.min).then_inc(route_pos, 1)
            dve.wait_ge(route_mm, 2 * NT)
            v.tensor_copy(slot_tok[:, :], bank[2][:, 0:NSE]).then_inc(route_tok, 1)

            def m_gate(s, u):
                dve.wait_ge(m_sil, s + 1)
                v.tensor_tensor(act_m[:, u, :], sil[:, u, :], bank[3 + u][:, :], ALU.mult).then_inc(m_act, 1)

            def m_tcopy(s, u):
                dve.wait_ge(m_at, s + 1)
                v.tensor_copy(act_t[:, u, :, :].rearrange("p k n -> p (k n)"), bank[5][:, :]).then_inc(m_atc, 1)

            m_gate(0, 0)
            with dve.Fori(0, (NSLOT - 1) // 2) as i:
                for u in range(2):
                    s = i * 2 + u
                    m_gate(s + 1, 1 - u)
                    m_tcopy(s, u)
            for s in range((NSLOT - 1) // 2 * 2, NSLOT):
                if s + 1 < NSLOT:
                    m_gate(s + 1, (s + 1) % 2)
                m_tcopy(s, s % 2)

            for i in range(NT):
                dve.wait_ge(yc_in[i % 2], 32 * (i // 2 + 1))
                if i == 0:
                    dve.wait_ge(x12_in, NT)
                for c in range(2):
                    link(v.scalar_tensor_tensor(x_sb[:, i, :], yc[:, i % 2, c, :], gate[:, 2 + c, i:i + 1],
                                                x_sb[:, i, :], ALU.mult, ALU.add))
                link(v.bn_stats(stat6[:, i % 2, :], x_sb[:, i, :]))
                v.bn_aggr(mv[:, 3, i, :], stat6[:, i % 2, :]).then_inc(stats_in[3], 1)
                v.tensor_copy(gate[:, 0, 0:1], ln1_sb[:, 0:1]).then_inc(x3_in, 1)
                dve.wait_ge(rstd_in[3], i + 1)
                if i >= 2:
                    dve.wait_ge(c_tr, i - 1)
                normalise(hc[:, i % 2, :], 3, i, x_sb[:, i, :]).then_inc(c_h, 1)

            for st, init in ((o_st, -1e38), (p_st, 0.0), (q_st, 0.0)):
                last = v.memset(st[:, :, :, 0:1], init)
            link(last)
            for half in range(2):
                dve.wait_ge(c_kt, (half + 1) * NT // 2)
                for k in range(KC):
                    n = half * KC + k
                    key = h_t[:, k, half * HB * S:(half + 1) * HB * S].rearrange("p (b t) -> p b t", b=HB)
                    o0 = o_st[:, k, :, 0:S]
                    for b in range(HB):
                        last = v.tensor_tensor_scan(o_st[:, k, b, 1:S + 1],
                                                    decay_sb[:, k:k + 1].to_broadcast([P, S]), key[:, b, :],
                                                    -1e38, ALU.add, ALU.max)
                    link(last)
                    link(v.scalar_tensor_tensor(d_ok[:, k, :, :], o0, decay_sb[:, k:k + 1], key, ALU.add, ALU.subtract))
                    v.tensor_scalar(e_a2[:, k, :, :], d_ok[:, k, :, :], 0.0, None, ALU.min).then_inc(c_dok, 1)
                    v.tensor_scalar(e_e2[:, k, :, :], d_ok[:, k, :, :], -1.0, 0.0, ALU.mult, ALU.min).then_inc(c_dok, 1)
                    link(v.scalar_tensor_tensor(d_ou[:, k, :, :], key, bonus_sb[:, k:k + 1], o0, ALU.add, ALU.subtract))
                    v.tensor_scalar(e_a[:, k, :, :], d_ou[:, k, :, :], -1.0, 0.0, ALU.mult, ALU.min).then_inc(c_dou, 1)
                    v.tensor_scalar(e_e[:, k, :, :], d_ou[:, k, :, :], 0.0, None, ALU.min).then_inc(c_dou, 1)
                for k in range(KC):
                    n = half * KC + k
                    dve.wait_ge(c_ea2, n + 1)
                    for b in range(HB):
                        last = v.tensor_tensor_scan(q_st[:, k, b, 1:S + 1], e_a2[:, k, b, :], e_e2[:, k, b, :],
                                                    0.0, ALU.mult, ALU.add)
                    link(last)
                    dve.wait_ge(c_ev, 2 * n + 2)
                    for b in range(HB):
                        last = v.tensor_tensor_scan(p_st[:, k, b, 1:S + 1], e_a2[:, k, b, :], e_e2v[:, k, b, :],
                                                    0.0, ALU.mult, ALU.add)
                    link(last)
                    dve.wait_ge(c_ea, n + 1)
                    v.tensor_tensor(d_ok[:, k, :, :], e_a[:, k, :, :], q_st[:, k, :, 0:S], ALU.mult)
                    link(v.tensor_tensor(d_ou[:, k, :, :], e_a[:, k, :, :], p_st[:, k, :, 0:S], ALU.mult))
                    link(v.tensor_tensor(d_ok[:, k, :, :], d_ok[:, k, :, :], e_e[:, k, :, :], ALU.add))
                    v.tensor_tensor(d_ou[:, k, :, :], d_ou[:, k, :, :], e_ev[:, k, :, :], ALU.add)
                    link(v.reciprocal(d_ok[:, k, :, :], d_ok[:, k, :, :]))
                    if half >= 1:
                        dve.wait_ge(c_ytr, half * NT // 2)
                    v.tensor_tensor(wkv_t[:, k, :, :], d_ou[:, k, :, :], d_ok[:, k, :, :], ALU.mult).then_inc(c_y, 1)

                for i in range(half * NT // 2, (half + 1) * NT // 2):
                    dve.wait_ge(c_ytr, i + 1)
                    link(v.tensor_tensor(x_sb[:, i, :], bank[i % 2][:, 0:D], x_sb[:, i, :], ALU.add))
                    link(v.bn_stats(stat6[:, i % 2, :], x_sb[:, i, :]))
                    v.bn_aggr(mv[:, 4, i, :], stat6[:, i % 2, :]).then_inc(stats_in[4], 1)
                    v.tensor_copy(gate[:, 0, 0:1], ln1_sb[:, 0:1]).then_inc(x4_in, 1)

            def q_scales(j, i, src):
                s = q_s[:, j, i, :]
                link(v.tensor_reduce(s[:, 0:1], src, AX, ALU.max, apply_absolute_value=True))
                link(v.tensor_scalar(s[:, 0:1], s[:, 0:1], EPS, None, ALU.max))
                link(v.reciprocal(s[:, 1:2], s[:, 0:1]))
                v.tensor_scalar(s[:, 1:2], s[:, 1:2], 127.0, None, ALU.mult)
                link(v.tensor_scalar(s[:, 2:3], s[:, 0:1], 1.0 / 127.0, wmean[:, j:j + 1], ALU.mult, ALU.mult))

            def d_first(i):
                dve.wait_ge(rstd_in[4], i + 1)
                link(normalise(q_h[:, i % 2, :], 4, i, x_sb[:, i, :]))
                q_scales(0, i, q_h[:, i % 2, :])
                link(v.tensor_scalar(q_r[:, i % 2, :], q_h[:, i % 2, :], q_s[:, 0, i, 1:2], MAGIC, ALU.mult, ALU.add))
                if i >= 2:
                    dve.wait_ge(d_htr, i - 1)
                v.tensor_scalar(q_hb[:, i % 2, :], q_r[:, i % 2, :], MAGIC, 127.0, ALU.subtract, ALU.min)\
                    .then_inc(d_hb, 1)
                dve.wait_ge(d_htr, i + 1)
                if i >= 2:
                    dve.wait_ge(d_up, i - 1)
                v.tensor_copy(q_ht[:, i % 2, :, :].rearrange("p k n -> p (k n)"), bank[5][:, 0:P].bitcast(BF))\
                    .then_inc(d_htc, 1)

            def d_last(i):
                dve.wait_ge(d_down, i + 1)
                if i >= 2:
                    dve.wait_ge(out_done[i % 2], 16 * (i // 2))
                v.scalar_tensor_tensor(x_out[:, i % 2, :], bank[6 + i % 2][:, 0:D], q_s[:, 1, i, 2:3],
                                       x_sb[:, i, :], ALU.mult, ALU.add).then_inc(d_out, 1)

            d_first(0)
            for i in range(NT):
                if i + 1 < NT:
                    d_first(i + 1)
                dve.wait_ge(d_gelu, i + 1)
                q_scales(1, i, q_g[:, i % 2, :])
                link(v.tensor_scalar(q_g[:, i % 2, :], q_g[:, i % 2, :], q_s[:, 1, i, 1:2], MAGIC, ALU.mult, ALU.add))
                if i >= 2:
                    dve.wait_ge(d_gtr, i - 1)
                v.tensor_scalar(q_gb[:, i % 2, :], q_g[:, i % 2, :], MAGIC, 127.0, ALU.subtract, ALU.min)\
                    .then_inc(d_gb, 1)
                if i >= 1:
                    d_last(i - 1)
            d_last(NT - 1)

        @block.tensor
        def _(pe):
            t_ = nc.tensor

            def mm3(dst, l_hi, l_lo, r_hi, r_lo, start, stop):
                t_.matmul(dst, l_hi, r_hi, start=start, stop=False)
                t_.matmul(dst, l_hi, r_lo, start=False, stop=False)
                return t_.matmul(dst, l_lo, r_hi, start=False, stop=stop)

            def transpose_d(dst, src, chunks=KC, idt=None):
                for k in range(chunks):
                    last = t_.transpose(dst[:, k * P:(k + 1) * P], src[:, k * P:(k + 1) * P],
                                        ident[:, :] if idt is None else idt)
                return last

            def a_product(i, hi, lo, b0):
                for c in range(2):
                    for k in range(KC):
                        last = mm3(bank[b0 + c][:, :], hi[:, i % 2, k, :], lo[:, i % 2, k, :],
                                   ctx_hi[:, k, c * 512:(c + 1) * 512], ctx_lo[:, k, c * 512:(c + 1) * 512],
                                   start=(k == 0), stop=(k == KC - 1))
                return last

            def a_first(i):
                pe.wait_ge(a_h_in, i + 1)
                if i == 0:
                    pe.wait_ge(consts, 1)
                if i >= 1:
                    pe.wait_ge(a_lo_in, i)
                transpose_d(bank[4], a_h[:, i % 2, :]).then_inc(a_tr, 1)

            def a_upper(i):
                pe.wait_ge(a_lo_in, i + 1)
                if i == 0:
                    pe.wait_ge(ctx_lo_in, KC)
                if i >= 1:
                    pe.wait_ge(a_u_in, i)
                a_product(i, a_hi, a_lo, 0).then_inc(a_up, 1)

            a_first(0)
            a_upper(0)
            for i in range(NT):
                if i + 1 < NT:
                    a_first(i + 1)
                    a_upper(i + 1)
                pe.wait_ge(a_act_in, i + 1)
                if i >= 1:
                    pe.wait_ge(a_lo2_in, i)
                transpose_d(bank[5], a_act[:, i % 2, :]).then_inc(a_tr2, 1)
                pe.wait_ge(a_lo2_in, i + 1)
                if i >= 1:
                    pe.wait_ge(stats_in[1], i)
                a_product(i, a_acthi, a_actlo, 2).then_inc(a_down, 1)
                if i == 3:
                    pe.wait_ge(w_abs_in, 1)
                    t_.matmul(bank[7][:, 0:2], ones_f[:, :], wabs[:, :], start=True, stop=True).then_inc(w_tot, 1)

            pe.wait_ge(wqkv_scaled, 1)
            pe.wait_ge(w_scale_in, 1)
            for b in range(B):
                for t in range(TB):
                    i = b * TB + t
                    pe.wait_ge(b_xn, i + 1)
                    if i >= 1:
                        pe.wait_ge(b_ht, i)
                    transpose_d(bank[6], xn_b[:, i % 2, :]).then_inc(b_tr, 1)
                pe.wait_ge(b_ht, TB * (b + 1))
                for qk in range(2):
                    if b >= 1:
                        pe.wait_ge(b_lo, 2 * (b - 1) + qk + 1)
                    for m in range(KC):
                        for k in range(KC):
                            last = t_.matmul(bank[7 if qk == 0 else 0][:, m * S:(m + 1) * S],
                                             wqkv[:, k, qk * D + m * P:qk * D + (m + 1) * P],
                                             h_t[:, k, b * S:(b + 1) * S], start=(k == 0), stop=(k == KC - 1))
                    last.then_inc(b_qk, 1)

            def v_proj(b):
                for t in range(TB):
                    for k in range(KC):
                        last = t_.matmul(bank[1][:, t * D:(t + 1) * D], h_t[:, k, b * S + t * P:b * S + (t + 1) * P],
                                         wqkv[:, k, 2 * D:3 * D], start=(k == 0), stop=(k == KC - 1))
                last.then_inc(b_v, 1)

            def score_rows(m):
                b, h = where(m)
                if h == 0:
                    pe.wait_ge(pack_in[b], 192)
                if m >= 2:
                    pe.wait_ge(max_done, m - 1)
                r = slice(64 * (h % 2), 64 * (h % 2) + 3 * HD)
                q, k = q_pack[b % 2], k_pack[b % 2]
                dst = bank[2 + h % 2]
                for t in range(TB):
                    last = t_.matmul(dst[:, t * P:t * P + (t + 1) * P], q[r, h // 2, t * P:(t + 1) * P],
                                     k[r, h // 2, 0:(t + 1) * P], start=True, stop=True)
                last.then_inc(s_done, 1)

            def max_rows(b):
                pe.wait_ge(max_done, H * (b + 1))
                for t in range(TB):
                    last = t_.transpose(bank[1][0:H, t * P:(t + 1) * P], negmax[:, b % 2, t, :], ident[:, :])
                last.then_inc(nm_tr, 1)

            def score_cols(n):
                b, h = where(n)
                if h == 0:
                    pe.wait_ge(nm_in[b], 32)
                if n >= 3:
                    pe.wait_ge(exp_done, n - 2)
                r = slice(64 * (h % 2), 64 * (h % 2) + 3 * HD + 1)
                q, k = q_pack[b % 2], k_pack[b % 2]
                dst = bank[4 + n % 3]
                t_.matmul(dst[:, 0:S], k[r, h // 2, 0:P], q[r, h // 2, :], start=True, stop=True)
                t_.matmul(dst[:, S:S + P], k[r, h // 2, P:S], q[r, h // 2, P:S], start=True, stop=True)\
                    .then_inc(st_done, 1)

            def weighted_values(n):
                b, h = where(n)
                pe.wait_ge(mask_done, n + 1)
                if h == 0:
                    pe.wait_ge(b_vaug, b + 1)
                if n % 4 == 0 and n >= 4:
                    pe.wait_ge(o_copied, n // 4)
                r = slice(32 * (h % 4), 32 * (h % 4) + 32)
                E = E_sb[:, n % 3, :]
                t_.matmul(bank[7][r, 0:S], v_aug[:, b % 2, 0, h, :], E[:, 0:S], start=True, stop=False)
                t_.matmul(bank[7][r, P:S], v_aug[:, b % 2, 1, h, :], E[:, S:S + P], start=False, stop=True)\
                    .then_inc(av_done, 1)

            pe.wait_ge(b_lo, 2 * B)
            v_proj(0)
            for m in range(H):
                score_rows(m)
            pe.wait_ge(b_vaug, 1)
            max_rows(0)
            for n in range(NSTEP + H):
                b, h = where(n)
                if n < NSTEP:
                    score_cols(n)
                if 1 <= n <= NSTEP:
                    weighted_values(n - 1)
                if b >= 1:
                    for t in range(TB):
                        i = (b - 1) * TB + t
                        if h == EP_OT[t]:
                            pe.wait_ge(o_copied, 4 * b)
                            if i >= 1:
                                pe.wait_ge(ep_h, i)
                            if i >= 2:
                                pe.wait_ge(ep_lgc, i if t == 0 else i - 1)
                            for gr in range(H // 4):
                                last = t_.transpose(bank[0][:, gr * P:(gr + 1) * P], o_t[:, gr, t * P:(t + 1) * P],
                                                    ident[:, :])
                            last.then_inc(ep_ot, 1)
                        if h == EP_HT[t]:
                            pe.wait_ge(ep_h, i + 1)
                            if i >= 1:
                                pe.wait_ge(stats_in[2], i)
                            pe.wait_ge(b_vaug, min(b + 1, B))
                            pe.wait_ge(nm_row, min(b + 1, B))
                            transpose_d(bank[1], h_tok[:, t, :]).then_inc(ep_ht, 1)
                        if h == EP_WO[t]:
                            pe.wait_ge(ep_htc, i + 1)
                            for k in range(KC):
                                last = t_.matmul(bank[1][:, D:2 * D], ho_t[:, t, k, :], wo[:, k, :],
                                                 start=(k == 0), stop=(k == KC - 1))
                            last.then_inc(ep_wo, 1)
                        if h == EP_XT[t]:
                            pe.wait_ge(ep_xn, i + 1)
                            pe.wait_ge(ep_h, b * TB)
                            if i >= 1:
                                pe.wait_ge(ep_lgc, i)
                            transpose_d(bank[0], x2_n[:, i % 2, :]).then_inc(ep_xt, 1)
                        if h == EP_LG[t]:
                            pe.wait_ge(ep_xtc, i + 1)
                            for k in range(KC):
                                last = t_.matmul(bank[0][:, D:D + NE], x2_t[:, t, k, :], wr[:, k, :],
                                                 start=(k == 0), stop=(k == KC - 1))
                            last.then_inc(ep_lg, 1)
                if n < NSTEP and b + 1 < B:
                    if S_FIRST <= h < S_FIRST + H // 2:
                        for j in range(2):
                            score_rows((b + 1) * H + 2 * (h - S_FIRST) + j)
                    if h == V_STEP:
                        pe.wait_ge(stats_in[2], TB * b)
                        v_proj(b + 1)
                    if h == NM_STEP:
                        pe.wait_ge(b_vaug, b + 2)
                        max_rows(b + 1)

            pe.wait_ge(picked_in, 1)
            flat = picked[:, :, :].rearrange("p i e -> p (i e)")
            t_.matmul(bank[1][:, 0:(NT + 1) * NE], earlier[:, :], flat, start=True, stop=False)
            for i in range(NT):
                reps = NT - i
                last = t_.matmul(bank[1][:, (i + 1) * NE:(NT + 1) * NE].rearrange("p (i e) -> p i e", i=reps),
                                 ones_b[:, :], picked[:, i:i + 1, :].to_broadcast([P, reps, NE]),
                                 start=False, stop=(i == NT - 1))
            last.then_inc(ranks, 1)
            for n in range(2 * NT):
                pe.wait_ge(route_oh, n + 1)
                t_.matmul(bank[2][:, 0:NSE], slot_oh[:, n % 4, :], slot_val[:, n % 4, :],
                          start=(n == 0), stop=(n == 2 * NT - 1)).then_inc(route_mm, 1)

            def m_transpose(s, u, turn):
                pe.wait_ge(xg_in[u], turn * 16)
                transpose_d(bank[0], xg[:, u, :]).then_inc(m_tr, 1)

            def m_up(s, u):
                e = pe.value_load(slot_e[0:1, bass.ds(s, 1)], min_val=0, max_val=NE - 1)
                pe.wait_ge(m_xt, s + 1)
                for c in range(2):
                    for k in range(KC):
                        last = t_.matmul(bank[1 + 2 * c + u][:, :], xg_t[:, u, k, :],
                                         we_sb[:, bass.ds(e * WE + (k * 2 + c) * INTER, INTER)],
                                         start=(k == 0), stop=(k == KC - 1))
                last.then_inc(m_gu, 1)

            def m_down(s, u):
                pe.wait_ge(m_act, s + 1)
                transpose_d(bank[5], act_m[:, u, :], chunks=IC).then_inc(m_at, 1)
                e = pe.value_load(slot_e[0:1, bass.ds(s, 1)], min_val=0, max_val=NE - 1)
                pe.wait_ge(m_atc, s + 1)
                for j in range(IC):
                    last = t_.matmul(bank[6 + u][:, 0:D], act_t[:, u, j, :],
                                     we_sb[:, bass.ds(e * WE + 2 * KC * INTER + j * D, D)],
                                     start=(j == 0), stop=(j == IC - 1))
                last.then_inc(m_y, 1)

            pe.wait_ge(in_experts, 16 * NE)
            pe.wait_ge(route_pos, 1)
            m_transpose(0, 0, 1)
            pe.wait_ge(m_xt, 1)
            m_transpose(1, 1, 1)
            m_up(0, 0)

            def m_iteration(s, u, turn, first):
                if first != 0:
                    pe.wait_ge(m_act, s)
                m_up(s + 1, 1 - u)
                pe.wait_ge(m_xt, s + 2)
                m_transpose(s + 2, u, turn)
                if first >= 2:
                    pe.wait_ge(m_yc, s - 1)
                m_down(s, u)

            for s in range(2):
                m_iteration(s, s, 2, s)
            with pe.Fori(1, (NSLOT - 3) // 2) as i:
                for u in range(2):
                    m_iteration(i * 2 + u, u, i + 2, 2)
            for s in range((NSLOT - 3) // 2 * 2, NSLOT):
                if s + 2 < NSLOT:
                    m_iteration(s, s % 2, s // 2 + 2, 2)
                else:
                    if s + 1 < NSLOT:
                        pe.wait_ge(m_act, s)
                        m_up(s + 1, (s + 1) % 2)
                    pe.wait_ge(m_yc, s - 1)
                    m_down(s, s % 2)

            for i in range(NT):
                pe.wait_ge(c_h, i + 1)
                if i >= 2:
                    pe.wait_ge(c_kt, i - 1)
                transpose_d(bank[i % 2], hc[:, i % 2, :]).then_inc(c_tr, 1)
            for i in range(NT):
                half = i // (NT // 2)
                pe.wait_ge(c_y, KC * (half + 1))
                pe.wait_ge(c_kt, NT)
                if i >= 2:
                    pe.wait_ge(x4_in, i - 1)
                bb, tt = (i % (NT // 2)) // TB, i % TB
                for k in range(KC):
                    last = t_.transpose(bank[i % 2][:, k * P:(k + 1) * P], wkv_t[:, k, bb, tt * P:(tt + 1) * P],
                                        ident[:, :])
                last.then_inc(c_ytr, 1)

            def d_first(i):
                pe.wait_ge(d_hb, i + 1)
                if i >= 1:
                    pe.wait_ge(d_htc, i)
                psb = bank[5][:, 0:P].bitcast(BF)
                transpose_d(psb, q_hb[:, i % 2, :], idt=ident_b[:, :]).then_inc(d_htr, 1)
                pe.wait_ge(d_htc, i + 1)
                if i >= 1:
                    pe.wait_ge(d_gelu, i)
                for c in range(2):
                    for k in range(KC):
                        last = t_.matmul(bank[2 + c][:, :], q_ht[:, i % 2, k, :], w1q[:, k, c * 512:(c + 1) * 512],
                                         start=(k == 0), stop=(k == KC - 1))
                last.then_inc(d_up, 1)

            pe.wait_ge(w_quant, 1)
            d_first(0)
            for i in range(NT):
                if i + 1 < NT:
                    d_first(i + 1)
                pe.wait_ge(d_gb, i + 1)
                if i >= 1:
                    pe.wait_ge(d_gtc, i)
                transpose_d(bank[4][:, :].bitcast(BF), q_gb[:, i % 2, :], chunks=FC, idt=ident_b[:, :])\
                    .then_inc(d_gtr, 1)
                pe.wait_ge(d_gtc, i + 1)
                if i >= 2:
                    pe.wait_ge(d_out, i - 1)
                for j in range(FC):
                    last = t_.matmul(bank[6 + i % 2][:, 0:D], q_gt[:, i % 2, j, :], w2q[:, j, :],
                                     start=(j == 0), stop=(j == FC - 1))
                last.then_inc(d_down, 1)


def kernel(**inputs):
    import numpy as np
    import concourse.bacc as bacc
    from concourse.bass_utils import run_bass_kernel_spmd

    def arr(name):
        return np.asarray(inputs[name])

    P, D = 128, 256
    x = arr("x")
    wg, wu, wd = arr("L0_ffn_Wg"), arr("L0_ffn_Wu"), arr("L0_ffn_Wd")
    NE, INTER = wg.shape[0], wg.shape[1]
    up = np.stack([wg.transpose(0, 2, 1), wu.transpose(0, 2, 1)], axis=2).reshape(NE, D // P, P, 2 * INTER)
    up = up.transpose(0, 2, 1, 3).reshape(NE, P, -1)
    down = wd.transpose(0, 2, 1).reshape(NE, INTER // P, P, D).transpose(0, 2, 1, 3).reshape(NE, P, -1)
    col = lambda a: a.reshape(D // P, P).T
    w1, w2 = arr("L1_ffn_w1"), arr("L1_ffn_w2")
    laid = {
        "x": x.reshape(-1, D),
        "ids": arr("itok_BxS_13_99985").reshape(-1, P).T,
        "ctx_t": arr("ctx_2048").transpose(2, 0, 1),
        "wqkv_t": np.concatenate([arr("L0_ffn_Wq").T, arr("L0_ffn_Wk").T, arr("L0_ffn_Wv").T], axis=1),
        "wo_t": arr("L0_ffn_Wo").T,
        "wr_t": arr("L0_ffn_Wr").T,
        "wexp": np.concatenate([up, down], axis=2),
        "ln1": col(arr("L0_ffn_w_ln1")),
        "ln2": col(arr("L0_ffn_w_ln2")),
        "decay": col(arr("L1_xattn_w")),
        "bonus": col(arr("L1_xattn_u")),
        "w1_t": w1.T.reshape(D // P, P, w1.shape[0]),
        "w2_t": w2.T.reshape(w2.shape[1] // P, P, D),
    }
    nc = bacc.Bacc("TRN2", target_bir_lowering=False, num_devices=1, dynamic_dma_scratch_size=8192)
    arrays, args = {}, []
    for name, a in laid.items():
        a = np.ascontiguousarray(a)
        arrays[f"in_{name}"] = a
        args.append(nc.dram_tensor(f"in_{name}", a.shape, mybir.dt.from_np(a.dtype), kind="ExternalInput").ap())
    out = nc.dram_tensor("out", (x.shape[0] * x.shape[1], D), mybir.dt.float32, kind="ExternalOutput").ap()
    mixed_block_kernel(nc, *args, out)
    r = run_bass_kernel_spmd(nc, [arrays], core_ids=[0])
    return r.results[0]["out"].reshape(x.shape)
```
